# Optimizing a Trainium2 kernel written in Bass

```python
import numpy as np
import jax
import jax.numpy as jnp

def _softmax(x, axis=-1):
    return jax.nn.softmax(x, axis=axis)

def _gelu(x):
    return jax.nn.gelu(x, approximate=True)

def _silu(x):
    return jax.nn.silu(x)

def _sigmoid(x):
    return jax.nn.sigmoid(x)

def _layernorm(x, axis=-1, eps=1e-05):
    m = jnp.mean(x, axis=axis, keepdims=True)
    v = jnp.var(x, axis=axis, keepdims=True)
    return (x - m) / jnp.sqrt(v + eps)

def _scatter_add(tgt, idx, src, axis=0):
    return tgt.at[idx].add(src)

def _segment_sum(src, seg, n):
    return jax.ops.segment_sum(src, seg, n)
kernel_name = 'mk_conv_preact_d2_conv_nchw1024_r2_dc38d5'

def setup_inputs(seed: int=0):
    np.random.seed(seed)
    _w = jnp.asarray

    def _rec_inputs():
        import jax
        import jax.numpy as jnp
        _gk = jax.random.key(seed)
        x = -0.000125 + 0.9999 * jax.random.normal(jax.random.fold_in(_gk, 1), (8, 512, 32, 32), jnp.float32)
        return x
    x = _rec_inputs()

    def _L0_conv_setup():
        import jax, jax.numpy as jnp
        import numpy as np
        CS = 5
        PAD = CS // 2
        EPS = 1e-12
        key = jax.random.key(seed)
        k1, k2, k3 = jax.random.split(key, 3)
        B, C, H, W = (8, 512, 32, 32)
        OC, INC = (512, C + CS * CS)
        feature = jax.random.normal(k1, (B, C, H, W), dtype=jnp.float32)
        conv_w = jax.random.normal(k2, (OC, INC), dtype=jnp.float32) * 0.02
        conv_b = jax.random.normal(k3, (OC,), dtype=jnp.float32) * 0.02
        return {'feature': feature, 'conv_w': conv_w, 'conv_b': conv_b}
    _L0_conv_all = _L0_conv_setup()
    _L0_conv_in = {k: v for k, v in _L0_conv_all.items() if k in ('conv_w', 'conv_b')}
    del _L0_conv_all

    def _L1_conv_setup():
        import jax, jax.numpy as jnp
        import numpy as np
        K = 5
        PAD = K // 2
        EPS = 1e-12
        key = jax.random.key(seed)
        k1, k2, k3 = jax.random.split(key, 3)
        b, c, h, w = (8, 512, 32, 32)
        out_ch = 512
        feature = jax.random.normal(k1, (b, c, h, w), dtype=jnp.float32)
        conv_w = jax.random.normal(k2, (out_ch, c + K * K), dtype=jnp.float32) * 0.02
        conv_b = jax.random.normal(k3, (out_ch,), dtype=jnp.float32) * 0.02
        return {'feature': feature, 'conv_w': conv_w, 'conv_b': conv_b}
    _L1_conv_all = _L1_conv_setup()
    _L1_conv_in = {k: v for k, v in _L1_conv_all.items() if k in ('conv_w', 'conv_b')}
    del _L1_conv_all
    return {'x': x, 'L0_conv_conv_w': _L0_conv_in['conv_w'], 'L0_conv_conv_b': _L0_conv_in['conv_b'], 'L1_conv_conv_w': _L1_conv_in['conv_w'], 'L1_conv_conv_b': _L1_conv_in['conv_b']}

def reference(x, L0_conv_conv_w, L0_conv_conv_b, L1_conv_conv_w, L1_conv_conv_b):
    import jax
    import jax.numpy as jnp

    def _L0_conv_ref(feature, conv_w, conv_b):
        import jax, jax.numpy as jnp
        import numpy as np
        CS = 5
        PAD = CS // 2
        EPS = 1e-12
        b, c, h, w = feature.shape
        norm = jnp.sqrt(jnp.sum(feature * feature, axis=1, keepdims=True))
        fn = feature / jnp.maximum(norm, EPS)
        fp = jnp.pad(fn, ((0, 0), (0, 0), (PAD, PAD), (PAD, PAD)))
        sims = []
        for cc in range(CS):
            for r in range(CS):
                sims.append(jnp.sum(fp[:, :, r:h + r, cc:w + cc] * fn, axis=1))
        vol = jnp.stack(sims, axis=1)
        x = jnp.concatenate([feature, vol], axis=1)
        out = jnp.einsum('bihw,oi->bohw', x, conv_w) + conv_b[None, :, None, None]
        return jax.nn.relu(out)

    def _L1_conv_ref(feature, conv_w, conv_b):
        import jax, jax.numpy as jnp
        import numpy as np
        K = 5
        PAD = K // 2
        EPS = 1e-12
        b, c, h, w = feature.shape
        norm = jnp.sqrt(jnp.sum(feature * feature, axis=1, keepdims=True))
        fn = feature / jnp.maximum(norm, EPS)
        fp = jnp.pad(fn, ((0, 0), (0, 0), (PAD, PAD), (PAD, PAD)))
        corr = jnp.stack([jnp.sum(fp[:, :, r:h + r, cc:w + cc] * fn, axis=1) for cc in range(K) for r in range(K)], axis=1)
        cat = jnp.concatenate([feature, corr], axis=1)
        y = jnp.einsum('oc,bchw->bohw', conv_w, cat) + conv_b[None, :, None, None]
        return jax.nn.relu(y)

    def _gn(v, G=32, eps=1e-05):
        B_, C_, H_, W_ = v.shape
        g = v.reshape(B_, G, C_ // G, H_, W_)
        m = jnp.mean(g, axis=(2, 3, 4), keepdims=True)
        s = jnp.var(g, axis=(2, 3, 4), keepdims=True)
        return ((g - m) / jnp.sqrt(s + eps)).reshape(v.shape)

    def _ln_c(v, eps=1e-06):
        m = jnp.mean(v, axis=1, keepdims=True)
        s = jnp.var(v, axis=1, keepdims=True)
        return (v - m) / jnp.sqrt(s + eps)

    def _ln_t(v, eps=1e-05):
        m = jnp.mean(v, axis=-1, keepdims=True)
        s = jnp.var(v, axis=-1, keepdims=True)
        return (v - m) / jnp.sqrt(s + eps)

    def _to_tokens(v):
        B_, C_, H_, W_ = v.shape
        return v.reshape(B_, C_, H_ * W_).transpose(0, 2, 1)

    def _from_tokens(t, like):
        B_, C_, H_, W_ = like.shape
        return t.transpose(0, 2, 1).reshape(B_, C_, H_, W_)
    x = x + _L0_conv_ref(_gn(x), L0_conv_conv_w, L0_conv_conv_b)
    x = x + _L1_conv_ref(_gn(x), L1_conv_conv_w, L1_conv_conv_b)
    return x

_drawn_inputs = setup_inputs


def setup_inputs(seed=0):
    import zlib

    import numpy as np

    out = dict(_drawn_inputs(seed))
    spreads = {}
    factors = {'L0_conv_conv_b': 4.569, 'L1_conv_conv_b': 4.788}
    for name, (base, spread) in spreads.items():
        noise = np.random.default_rng([zlib.crc32(name.encode()), seed]).standard_normal(out[name].shape)
        drawn = base * np.exp(spread * noise) if base else spread * noise
        out[name] = jnp.asarray(drawn.astype(out[name].dtype))
    for name, factor in factors.items():
        out[name] = (out[name] * factor).astype(out[name].dtype)
    return out
```

```python
from contextlib import ExitStack

import concourse.bass as bass
from concourse import mybir

ALU = mybir.AluOpType
ACT = mybir.ActivationFunctionType
AX = mybir.AxisListType
F32 = mybir.dt.float32
F16 = mybir.dt.float16
I32 = mybir.dt.int32

P = 128
HALF = 512

BATCHES, LAYERS = 8, 2
UNITS = BATCHES * LAYERS
LEAD = 2
RING = 4

V_SCALE = 256.0
W_SCALE = 1024.0


def unit_layer(u):
    if u <= LEAD:
        return 0
    return 1 if u % 2 or u > UNITS - LEAD - 2 else 0


def unit_batch(u):
    if u <= LEAD:
        return u
    if unit_layer(u) == 0:
        return (u + LEAD) // 2
    return (u - LEAD - 1) // 2 if u < UNITS - LEAD else u - BATCHES


ORDER = [(unit_layer(u), unit_batch(u)) for u in range(UNITS)]
assert sorted(ORDER) == [(l, b) for l in range(LAYERS) for b in range(BATCHES)]

FIRST_LOOPED, PERIOD, TRIPS = 3, 4, 2
LAST_LOOPED = FIRST_LOOPED + PERIOD * TRIPS - 1
for _k in range(FIRST_LOOPED - 1, FIRST_LOOPED + PERIOD + 1):
    for _i in range(TRIPS):
        assert unit_layer(_k + PERIOD * _i) == unit_layer(_k)
        assert unit_batch(_k + PERIOD * _i) == unit_batch(_k) + _i * PERIOD // 2


def build(nc, x, w0, b0, w1, b1, out):
    B, C, HI, WI = x.shape
    PIX = HI * WI
    KT = C // P
    CI = w0.shape[1]
    S = 5
    R = S // 2
    NS = S * S
    GROUP = C // 32
    ROWS = P // WI
    BLOCKS = PIX // P
    BAND = (ROWS + 2 * R) * WI
    PAIRS = BLOCKS // 2
    REACH = 2 * R * WI + S
    CENTRE = R * WI + R
    SPAN = HALF // WI
    PW = WI + 2 * R
    PSZ = PW * (HI + 2 * R)
    BACK = 64
    NROWS = BACK + NS + 1
    MIR = (HI - 1) * PW + WI
    GPAD = 64
    GSZ = GPAD + BLOCKS * P * BAND + GPAD
    GROUPS = 2 * KT
    BN = 6
    assert (B, UNITS) == (BATCHES, B * LAYERS) and BAND * 2 == HALF

    weights = (w0, w1)
    biases = (b0, b1)
    x_v = x.rearrange("b (t p) h w -> b p t (h w)", p=P)
    out_v = out.rearrange("b (t p) h w -> b p t (h w)", p=P)

    ctx = ExitStack()
    with ctx:
        def sb(name, shape, dt):
            return ctx.enter_context(nc.sbuf_tensor(name, shape, dt))

        def ps(name, shape, dt):
            return ctx.enter_context(nc.psum_tensor(name, shape, dt))

        def sem(name):
            return ctx.enter_context(nc.semaphore(name))

        band_dram = nc.dram_tensor("band_dram", (2, GSZ), F32)
        rows_dram = nc.dram_tensor("rows_dram", (2, (NS + 1) * PSZ), F32)

        xs = sb("xs", [P, RING, KT, PIX], F32)
        opnd = sb("opnd", [P, RING, 2, KT, PIX], F16)
        wh = sb("wh", [P, LAYERS, KT, C], F16)
        whh = sb("whh", [P, LAYERS, KT, C], F16)
        wl = sb("wl", [P, LAYERS, KT, C], F16)
        wvol = sb("wvol", [P, LAYERS, C], F16)
        vol = sb("vol", [P, PIX], F16)
        v2 = sb("v2", [P, 2, PIX], F32)
        band = sb("band", [P, PAIRS, HALF], F32)
        skew = sb("skew", [P, BLOCKS, REACH], F32)
        nbr = sb("nbr", [P, BLOCKS, NROWS], F32)
        rows = sb("rows", [NROWS, PSZ], F32)
        mirror = sb("mirror", [NS, HI * PW], F32)
        rn_far = sb("rn_far", [NS, HI * PW], F32)
        rn_own = sb("rn_own", [NS, HI * PW], F32)
        corr = sb("corr", [NS, PIX], F32)
        act_out = sb("act_out", [P, 2, HALF], F32)
        ident = sb("ident", [P, P], F32)
        avg = sb("avg", [P, P], F32)
        stats = sb("stats", [P, KT, 2, BN], F32)
        mv = sb("mv", [P, KT, 2], F32)
        gmv = sb("gmv", [P, KT, 2], F32)
        gvar = sb("gvar", [P, KT], F32)
        gstd = sb("gstd", [P, KT], F32)
        grs = sb("grs", [P, KT], F32)
        gtmp = sb("gtmp", [P, KT], F32)
        affine = sb("affine", [P, 2, 2, KT], F32)
        nsq = sb("nsq", [P, BLOCKS], F32)
        nrm = sb("nrm", [P, BLOCKS], F32)
        rn0 = sb("rn0", [P, BLOCKS], F32)
        rtmp = sb("rtmp", [P, BLOCKS], F32)
        rn = sb("rn", [P, BLOCKS], F32)
        carrier = sb("carrier", [P, 16], F32)
        wmax = sb("wmax", [P, LAYERS, KT], F32)
        wup = sb("wup", [P, LAYERS, KT], F32)
        wdown = sb("wdown", [P, LAYERS, KT], F32)
        bias = sb("bias", [P, LAYERS, KT], F32)
        w_raw = [opnd[:, RING - LAYERS + l, :, :, :].rearrange("p a t n -> p (a t n)").bitcast(F32)
                 [:, 0:KT * CI].rearrange("p (t n) -> p t n", t=KT) for l in range(LAYERS)]

        conv_ps = ps("conv_ps", [P, 4, HALF], F32)
        gram_ps = ps("gram_ps", [P, 2, HALF], F32)
        turn_ps = ps("turn_ps", [P, 2, HALF], F32)

        const_step = sem("const_step")
        pads_out = sem("pads_out")
        w_in = [sem(f"w_in{l}") for l in range(LAYERS)]
        x_in = [[sem(f"x_in{q}_{t}") for t in range(KT)] for q in range(2)]
        x_out = [sem(f"x_out{t}") for t in range(KT)]
        w_step = sem("w_step")
        w_turned = sem("w_turned")
        w_high = sem("w_high")
        w_half = sem("w_half")
        w_low = sem("w_low")
        bn_step = sem("bn_step")
        group_avg = sem("group_avg")
        gn_step = sem("gn_step")
        gn_root = sem("gn_root")
        high = sem("high")
        twice = sem("twice")
        low = sem("low")
        gram = sem("gram")
        band_sb = sem("band_sb")
        band_out = sem("band_out")
        skew_in = sem("skew_in")
        rn_step = sem("rn_step")
        rn_root = sem("rn_root")
        turned = sem("turned")
        rows_v = sem("rows_v")
        rows_a = sem("rows_a")
        rows_out = sem("rows_out")
        mirror_in = sem("mirror_in")
        corr_step = sem("corr_step")
        vol_high = sem("vol_high")
        vol_low = sem("vol_low")
        conv = sem("conv")
        relu = sem("relu")
        x_sum = sem("x_sum")

        CONSTS = 11
        BN_STEPS = KT + KT + 2
        GN_STEPS = 11
        RN_STEPS = 8
        CORR_STEPS = 3
        W_STEPS = 6
        ON_VECTOR = (0, 1)
        W_HIGHS = KT + 2
        W_LOWS = KT + 1

        def wait(eng, s, value):
            if not isinstance(value, int) or value > 0:
                eng.wait_ge(s, value)

        def ring_slot(b):
            return b % RING

        def slots(eng, step):
            for k in range(-1, FIRST_LOOPED):
                step(k, k, 0)
            with eng.Fori(0, TRIPS) as i:
                for k0 in range(FIRST_LOOPED, FIRST_LOOPED + PERIOD):
                    step(k0 + PERIOD * i, k0, i)
            for k in range(LAST_LOOPED + 1, UNITS + 1):
                step(k, k, 0)

        def valid(u):
            return 0 <= u < UNITS

        block = ctx.enter_context(nc.Block())

        @block.sync
        def _(sp):
            def load(b, slot, q):
                for t in range(KT):
                    sp.dma_start(xs[:, slot, t, :], x_v[b, :, t, :]).then_inc(x_in[q][t], 16)

            def load_weights(l):
                sp.dma_start(w_raw[l], weights[l].rearrange("(t p) c -> p t c", p=P)).then_inc(w_in[l], 16)
                with nc.allow_non_contiguous_dma(reason="512 bias values, once"):
                    sp.dma_start(bias[:, l, :], biases[l].rearrange("(t p) -> p t", p=P)).then_inc(w_in[l], 16)

            load(0, 0, 0)
            load(1, 1, 1)
            for l in range(LAYERS):
                load_weights(l)
            sp.wait_ge(const_step, CONSTS)
            for q in range(2):
                sp.dma_start(band_dram[q:q + 1, 0:GPAD], rows[0:1, 0:GPAD]).then_inc(pads_out, 16)
                sp.dma_start(band_dram[q:q + 1, GSZ - GPAD:GSZ], rows[0:1, 0:GPAD]).then_inc(pads_out, 16)
            sp.wait_ge(pads_out, 64)
            sp.wait_ge(bn_step, BN_STEPS)
            load(2, 2, 0)

            def tile_out(k, k0, i, t):
                b = unit_batch(k0 - 1) + 2 * i
                sp.wait_ge(x_sum, GROUPS * (k - 1) + 2 * t + 2)
                sp.dma_start(out_v[b, :, t, :], xs[:, ring_slot(b), t, :]).then_inc(x_out[t], 16)

            def tile_in(k, k0, i, t):
                b_0 = unit_batch(k0 - 1)
                b = b_0 + 2 * i
                if b_0 + RING < BATCHES:
                    sp.wait_ge(x_out[t], 16 * (b + 1))
                    sp.dma_start(xs[:, ring_slot(b), t, :], x_v[b + RING, :, t, :]).then_inc(x_in[b_0 % 2][t], 16)

            def band_through_dram(k, q):
                for p in range(PAIRS):
                    sp.wait_ge(band_sb, PAIRS * k + p + 1)
                    dst = bass.AP(band_dram, q * GSZ + GPAD + 2 * p * P * BAND,
                                  [[BAND, P], [P * BAND, 2], [1, BAND]])
                    sp.dma_start(dst, band[:, p, :].rearrange("p (a n) -> p a n", a=2)).then_inc(band_out, 16)
                sp.wait_ge(band_out, 16 * PAIRS * (k + 1))
                src = bass.AP(band_dram, q * GSZ + GPAD - R, [[BAND + 1, P], [P * BAND, BLOCKS], [1, REACH]])
                sp.dma_start(skew[:, :, :], src).then_inc(skew_in, 16)

            def rows_to_dram(k, q):
                sp.wait_ge(rows_v, k + 1)
                sp.wait_ge(rows_a, k + 1)
                sp.dma_start(rows_dram[q:q + 1, :].rearrange("a (s n) -> (a s) n", s=NS + 1),
                             rows[BACK:NROWS, :]).then_inc(rows_out, 16)

            def views_from_dram(k, q):
                sp.wait_ge(rows_out, 16 * (k + 1))
                base = q * (NS + 1) * PSZ
                sp.dma_start(mirror[:, 0:MIR],
                             bass.AP(rows_dram, base, [[S * PSZ + 1, S], [PSZ + PW, S], [1, MIR]])
                             ).then_inc(mirror_in, 16)
                sp.dma_start(rn_far[:, 0:MIR],
                             bass.AP(rows_dram, base + NS * PSZ, [[1, S], [PW, S], [1, MIR]])
                             ).then_inc(mirror_in, 16)
                sp.dma_start(rn_own[:, 0:MIR],
                             bass.AP(rows_dram, base + NS * PSZ + R * PW + R, [[0, NS], [1, MIR]])
                             ).then_inc(mirror_in, 16)

            def step(k, k0, i):
                finished = valid(k0 - 1) and unit_layer(k0 - 1) == 1
                if valid(k0):
                    band_through_dram(k, k0 % 2)
                if k0 == 0:
                    sp.wait_ge(bn_step, 2 * BN_STEPS)
                    load(3, 3, 1)
                if finished:
                    tile_out(k, k0, i, 0)
                    tile_in(k, k0, i, 0)
                    tile_out(k, k0, i, 1)
                if valid(k0):
                    rows_to_dram(k, k0 % 2)
                if finished:
                    tile_in(k, k0, i, 1)
                if valid(k0):
                    views_from_dram(k, k0 % 2)
                if finished:
                    for t in range(2, KT):
                        tile_out(k, k0, i, t)
                        tile_in(k, k0, i, t)

            slots(sp, step)
            for t in range(KT):
                sp.wait_ge(x_out[t], 16 * BATCHES)

        @block.gpsimd
        def _(pool):
            pool.memset(ident[:, :], 0.0).then_inc(const_step, 1)
            pool.memset(avg[:, :], 1.0 / GROUP).then_inc(const_step, 1)
            pool.wait_ge(const_step, 2)
            pool.affine_select(out=ident[:, :], in_=ident[:, :], compare_op=ALU.not_equal, fill=1.0, base=0,
                               pattern=[[-1, P]], channel_multiplier=1).then_inc(const_step, 1)
            avg_v = avg[:, :].rearrange("p (g c) -> p g c", c=GROUP)
            pool.affine_select(out=avg_v, in_=avg_v, compare_op=ALU.is_ge, fill=0.0, base=0,
                               pattern=[[-GROUP, P // GROUP], [0, GROUP]], channel_multiplier=1
                               ).then_inc(const_step, 1)
            pool.wait_ge(const_step, 4)
            pool.affine_select(out=avg_v, in_=avg_v, compare_op=ALU.is_ge, fill=0.0, base=GROUP - 1,
                               pattern=[[GROUP, P // GROUP], [0, GROUP]], channel_multiplier=-1
                               ).then_inc(const_step, 1)
            pool.memset(rows[:, :], 0.0).then_inc(const_step, 1)
            pool.memset(band[:, 0, 0:R * WI], 0.0).then_inc(const_step, 1)
            pool.memset(band[:, PAIRS - 1, HALF - R * WI:HALF], 0.0).then_inc(const_step, 1)
            pool.memset(vol[:, :], 0.0).then_inc(const_step, 1)
            pool.memset(wvol[:, :, :], 0.0).then_inc(const_step, 1)
            pool.memset(nbr[:, :, NS:BACK], 0.0).then_inc(const_step, 1)
            for l in range(LAYERS):
                for t in range(KT):
                    pool.wait_ge(w_high, W_HIGHS * l + t + 1)
                    pool.tensor_scalar(whh[:, l, t, :], wh[:, l, t, :], 0.5, 1.0, ALU.mult, ALU.mult
                                       ).then_inc(w_half, 1)

        @block.tensor
        def _(pe):
            pe.wait_ge(const_step, CONSTS)

            def average(u):
                pe.wait_ge(bn_step, BN_STEPS * (u + 1))
                wait(pe, rows_v, u - 1)
                pe.matmul(turn_ps[:, 0, 0:2 * KT], avg[:, :], mv[:, :, :].rearrange("p t s -> p (t s)"),
                          start=True, stop=True).then_inc(group_avg, 1)

            def turn_weights(l):
                pe.wait_ge(w_step, W_STEPS * (l + 1))
                for t in range(KT):
                    wait(pe, w_low, W_LOWS * (l - 1) + t + 1)
                    for m in range(KT):
                        last = pe.transpose(conv_ps[:, t, m * P:(m + 1) * P],
                                            w_raw[l][:, m, t * P:(t + 1) * P], ident[:, :])
                    last.then_inc(w_turned, 1)
                wait(pe, w_low, W_LOWS * l)
                for m in range(KT):
                    last = pe.transpose(turn_ps[0:NS, 1, m * P:(m + 1) * P], w_raw[l][:, m, C:CI], ident[:, :])
                last.then_inc(w_turned, 1)

            def step(k, k0, i):
                if valid(k0):
                    slot = k0 % RING
                    pe.wait_ge(high, KT * (k + 1))
                    pe.wait_ge(low, KT * (k + 1))
                    for p in range(PAIRS):
                        wait(pe, band_sb, PAIRS * k + p - 1)
                        for j in range(2 * p, 2 * p + 2):
                            r0 = max(ROWS * j - R, 0)
                            r1 = min(ROWS * (j + 1) + R, HI)
                            at = (j % 2) * BAND + (r0 - (ROWS * j - R)) * WI
                            for t in range(KT):
                                for part in range(2):
                                    last = pe.matmul(gram_ps[:, p % 2, at:at + (r1 - r0) * WI],
                                                     opnd[:, slot, 0, t, j * P:(j + 1) * P],
                                                     opnd[:, slot, part, t, r0 * WI:r1 * WI],
                                                     start=(t == 0 and part == 0),
                                                     stop=(t == KT - 1 and part == 1))
                        last.then_inc(gram, 1)
                u0 = k0 - 1
                if valid(u0):
                    u = k - 1
                    l = unit_layer(u0)
                    slot = u0 % RING
                for g in range(GROUPS):
                    if valid(k0 + 1) and g == 2:
                        average(k + 1)
                    if k0 == 0 and g == 6:
                        pe.wait_ge(rows_a, 1)
                        for l in range(LAYERS):
                            turn_weights(l)
                        pe.wait_ge(w_high, W_HIGHS * LAYERS)
                        pe.wait_ge(w_half, KT * LAYERS)
                        pe.wait_ge(w_low, W_LOWS * LAYERS)
                    if valid(k0) and g == 5:
                        wait(pe, rn_step, RN_STEPS * (k + 1))
                        if valid(k0 + 1):
                            wait(pe, gn_step, GN_STEPS * (k + 1) + 1)
                        for j in range(BLOCKS):
                            last = pe.transpose(turn_ps[0:NROWS, j * P // HALF, j * P % HALF:j * P % HALF + P],
                                                nbr[:, j, :], ident[:, :])
                        last.then_inc(turned, 1)
                    if not valid(u0):
                        continue
                    m, n = g // 2, g % 2
                    wait(pe, relu, GROUPS * u + g - 3)
                    acc = conv_ps[:, g % 4, :]
                    cols = slice(n * HALF, (n + 1) * HALF)
                    outs = slice(m * P, (m + 1) * P)
                    for t in range(KT):
                        for w, part in ((wh, 0), (wl, 0), (whh, 1)):
                            pe.matmul(acc, w[:, l, t, outs], opnd[:, slot, part, t, cols],
                                      start=(t == 0 and w is wh), stop=False)
                    if g == 0:
                        pe.wait_ge(vol_high, 2 * (u + 1))
                        pe.wait_ge(vol_low, u + 1)
                    pe.matmul(acc, wvol[0:96, l, outs], vol[0:96, cols], start=False, stop=True).then_inc(conv, 1)

            slots(pe, step)

        @block.scalar
        def _(act):
            act.wait_ge(const_step, CONSTS)

            def high_weights(l):
                for t in range(KT):
                    act.wait_ge(w_turned, (KT + 1) * l + t + 1)
                    act.activation(wh[:, l, t, :], conv_ps[:, t, :], ACT.Copy).then_inc(w_high, 1)
                act.wait_ge(w_turned, (KT + 1) * (l + 1))
                for at in (0, 32):
                    act.activation(wvol[at:at + NS, l, :], turn_ps[0:NS, 1, :], ACT.Copy).then_inc(w_high, 1)

            def carry_act(at):
                act.activation(carrier[:, 8 + at:9 + at], ident[:, 0:1], ACT.Copy)

            def norm_tile(u, u0, i, t):
                xt = xs[:, ring_slot(unit_batch(u0) + 2 * i), t, :]
                act.activation(opnd[:, u0 % RING, 0, t, :], xt, ACT.Identity, bias=affine[:, 0, 1, t:t + 1],
                               scale=affine[:, 0, 0, t:t + 1]).then_inc(high, 1)
                if u0 in ON_VECTOR:
                    return
                wait(act, low, KT * u + t - 1)
                if not isinstance(u, int):
                    carry_act(t)
                act.activation(v2[:, t % 2, :], xt, ACT.Identity, bias=affine[:, 1, 1, t:t + 1],
                               scale=affine[:, 1, 0, t:t + 1]).then_inc(twice, 1)

            def volume_high(u):
                act.wait_ge(corr_step, CORR_STEPS * (u + 1))
                wait(act, conv, GROUPS * u)
                for at in (0, 64):
                    act.activation(vol[at:at + NS, :], corr[:, :], ACT.Copy, scale=V_SCALE / 2
                                   ).then_inc(vol_high, 1)

            def step(k, k0, i):
                u0, u = k0 - 1, k - 1
                for p in range(PAIRS):
                    if p == 2 and valid(u0):
                        volume_high(u)
                    if valid(k0):
                        act.wait_ge(gram, PAIRS * k + p + 1)
                        if p == 0:
                            wait(act, band_out, 16 * PAIRS * k)
                        a = R * WI if p == 0 else 0
                        z = HALF - (R * WI if p == PAIRS - 1 else 0)
                        act.activation(band[:, p, a:z], gram_ps[:, p % 2, a:z], ACT.Copy).then_inc(band_sb, 1)
                for g in range(GROUPS):
                    if g == 2 and valid(k0 + 1):
                        act.wait_ge(gn_step, GN_STEPS * (k + 1) + 4)
                        act.activation(gstd[:, :], gvar[:, :], ACT.Sqrt).then_inc(gn_root, 1)
                    if g == 2 and valid(k0):
                        act.wait_ge(rn_step, RN_STEPS * k + 1)
                        act.activation(nrm[:, :], nsq[:, :], ACT.Sqrt).then_inc(rn_root, 1)
                    if 2 <= g < 2 + KT and valid(k0 + 1):
                        if g == 2:
                            act.wait_ge(gn_step, GN_STEPS * (k + 2))
                        if k0 == 1:
                            act.wait_ge(w_turned, (KT + 1) * LAYERS)
                        norm_tile(k + 1, k0 + 1, i, g - 2)
                    if g == 7 and k0 == 0:
                        for l in range(LAYERS):
                            high_weights(l)
                    if g == 5 and valid(k0):
                        act.wait_ge(turned, k + 1)
                        wait(act, rows_out, 16 * k)
                        wait(act, corr_step, CORR_STEPS * k)
                        inner = rows[:, :].rearrange("s (h w) -> s h w", w=PW)[:, R + SPAN:R + 2 * SPAN, R:R + WI]
                        act.activation(inner, turn_ps[0:NROWS, 1, :].rearrange("s (h w) -> s h w", w=WI),
                                       ACT.Copy).then_inc(rows_a, 1)
                    if valid(u0):
                        l = unit_layer(u0)
                        m = g // 2
                        act.wait_ge(conv, GROUPS * u + g + 1)
                        wait(act, x_sum, GROUPS * u + g - 1)
                        act.activation(act_out[:, g % 2, :], conv_ps[:, g % 4, :], ACT.Relu,
                                       bias=bias[:, l, m:m + 1], scale=wdown[:, l, m:m + 1]).then_inc(relu, 1)

            slots(act, step)

        @block.vector
        def _(dve):
            dve.wait_ge(const_step, CONSTS)

            def carry_dve(at):
                dve.memset(carrier[:, at:at + 1], 0.0)

            def unit_stats(k, k0, i):
                u, u0 = k + 1, k0 + 1
                b_0 = unit_batch(u0)
                slot = ring_slot(b_0 + 2 * i)
                base = BN_STEPS * u
                if unit_layer(u0) == 1:
                    wait(dve, x_sum, GROUPS * (u - 2))
                    if not isinstance(u, int):
                        carry_dve(KT)
                for t in range(KT):
                    if t == 2 and valid(k0 - 1):
                        volume_low(k)
                    if unit_layer(u0) == 0:
                        dve.wait_ge(x_in[b_0 % 2][t], 16 * (b_0 // 2 + 1 + i))
                        if not isinstance(u, int):
                            carry_dve(t)
                    for h in range(2):
                        last = dve.bn_stats(stats[:, t, h, :], xs[:, slot, t, h * HALF:(h + 1) * HALF])
                    last.then_inc(bn_step, 1)
                if k0 >= 0:
                    dve.wait_ge(group_avg, u)
                wait(dve, bn_step, base + KT)
                if not isinstance(u, int):
                    carry_dve(KT + 1)
                for t in range(KT):
                    dve.bn_aggr(mv[:, t, :], stats[:, t, :, :].rearrange("p h s -> p (h s)")).then_inc(bn_step, 1)
                dve.wait_ge(bn_step, base + 2 * KT)
                dve.tensor_tensor(gtmp[:, :], mv[:, :, 0], mv[:, :, 0], ALU.mult).then_inc(bn_step, 1)
                dve.wait_ge(bn_step, base + 2 * KT + 1)
                dve.tensor_tensor(mv[:, :, 1], mv[:, :, 1], gtmp[:, :], ALU.add).then_inc(bn_step, 1)

            def unit_affine(k, k0):
                u = k + 1
                base = GN_STEPS * u
                dve.wait_ge(group_avg, u + 1)
                dve.tensor_copy(gmv[:, :, :].rearrange("p t s -> p (t s)"), turn_ps[:, 0, 0:2 * KT]
                                ).then_inc(gn_step, 1)
                dve.wait_ge(gn_step, base + 1)
                dve.tensor_tensor(gtmp[:, :], gmv[:, :, 0], gmv[:, :, 0], ALU.mult).then_inc(gn_step, 1)
                dve.wait_ge(gn_step, base + 2)
                dve.tensor_tensor(gvar[:, :], gmv[:, :, 1], gtmp[:, :], ALU.subtract).then_inc(gn_step, 1)
                dve.wait_ge(gn_step, base + 3)
                dve.tensor_scalar(gvar[:, :], gvar[:, :], 0.0, 1e-5, ALU.max, ALU.add).then_inc(gn_step, 1)
                dve.wait_ge(gn_root, u + 1)
                dve.reciprocal(grs[:, :], gstd[:, :]).then_inc(gn_step, 1)
                dve.wait_ge(gn_step, base + 5)
                dve.tensor_tensor(gtmp[:, :], grs[:, :], grs[:, :], ALU.mult).then_inc(gn_step, 1)
                dve.wait_ge(gn_step, base + 6)
                dve.tensor_tensor(gtmp[:, :], gtmp[:, :], gvar[:, :], ALU.mult).then_inc(gn_step, 1)
                dve.wait_ge(gn_step, base + 7)
                dve.tensor_scalar(gtmp[:, :], gtmp[:, :], -0.5, 1.5, ALU.mult, ALU.add).then_inc(gn_step, 1)
                dve.wait_ge(gn_step, base + 8)
                wait(dve, twice, KT * u)
                dve.scalar_tensor_tensor(out=affine[:, 0, 0, :], in0=grs[:, :], scalar=V_SCALE, in1=gtmp[:, :],
                                         op0=ALU.mult, op1=ALU.mult).then_inc(gn_step, 1)
                dve.wait_ge(gn_step, base + 9)
                dve.scalar_tensor_tensor(out=affine[:, 0, 1, :], in0=gmv[:, :, 0], scalar=-1.0,
                                         in1=affine[:, 0, 0, :], op0=ALU.mult, op1=ALU.mult).then_inc(gn_step, 1)
                dve.wait_ge(gn_step, base + 10)
                dve.tensor_scalar(affine[:, 1, :, :], affine[:, 0, :, :], 2.0, None, ALU.mult).then_inc(gn_step, 1)

            def low_tile(k, k0, t):
                u, slot = k + 1, (k0 + 1) % RING
                if k0 + 1 in ON_VECTOR:
                    dve.wait_ge(gn_step, GN_STEPS * (k + 2))
                    wait(dve, low, KT * u + t - 1)
                    dve.tensor_scalar(v2[:, t % 2, :], xs[:, ring_slot(unit_batch(k0 + 1)), t, :],
                                      affine[:, 1, 0, t:t + 1], affine[:, 1, 1, t:t + 1], ALU.mult, ALU.add
                                      ).then_inc(twice, 1)
                dve.wait_ge(high, KT * u + t + 1)
                dve.wait_ge(twice, KT * u + t + 1)
                dve.scalar_tensor_tensor(out=opnd[:, slot, 1, t, :], in0=opnd[:, slot, 0, t, :], scalar=-2.0,
                                         in1=v2[:, t % 2, :], op0=ALU.mult, op1=ALU.add).then_inc(low, 1)

            def correlation(k):
                u = k - 1
                base = CORR_STEPS * u
                own = rows[0:NS, :].rearrange("s (h w) -> s h w", w=PW)[:, R:R + HI, R:R + WI]
                mir, far, near = (a[:, :].rearrange("s (h w) -> s h w", w=PW)[:, :, 0:WI]
                                  for a in (mirror, rn_far, rn_own))
                dst = corr[:, :].rearrange("s (h w) -> s h w", w=WI)
                dve.wait_ge(mirror_in, 48 * (u + 1))
                dve.wait_ge(rows_a, u + 1)
                dve.tensor_tensor(mir, mir, near, ALU.mult).then_inc(corr_step, 1)
                wait(dve, vol_low, u)
                wait(dve, vol_high, 2 * u)
                dve.tensor_tensor(dst, own, far, ALU.mult).then_inc(corr_step, 1)
                dve.wait_ge(corr_step, base + 2)
                dve.tensor_tensor(dst, dst, mir, ALU.add).then_inc(corr_step, 1)

            def volume_low(k):
                u = k - 1
                dve.wait_ge(vol_high, 2 * u + 1)
                dve.scalar_tensor_tensor(out=vol[32:32 + NS, :], in0=corr[:, :], scalar=V_SCALE / 2,
                                         in1=vol[0:NS, :], op0=ALU.mult, op1=ALU.subtract).then_inc(vol_low, 1)

            def norms(k):
                base = RN_STEPS * k
                dve.wait_ge(skew_in, 16 * (k + 1))
                dve.tensor_scalar(nsq[:, :], skew[:, :, CENTRE], (V_SCALE * 1e-12) ** 2, None, ALU.max
                                  ).then_inc(rn_step, 1)

            def neighbours(k):
                base = RN_STEPS * k
                dve.wait_ge(rn_root, k + 1)
                dve.reciprocal(rn0[:, :], nrm[:, :]).then_inc(rn_step, 1)
                dve.wait_ge(rn_step, base + 2)
                dve.tensor_tensor(rtmp[:, :], rn0[:, :], rn0[:, :], ALU.mult).then_inc(rn_step, 1)
                dve.wait_ge(rn_step, base + 3)
                dve.tensor_tensor(rtmp[:, :], rtmp[:, :], nsq[:, :], ALU.mult).then_inc(rn_step, 1)
                dve.wait_ge(rn_step, base + 4)
                dve.tensor_scalar(rtmp[:, :], rtmp[:, :], -0.5, 1.5, ALU.mult, ALU.add).then_inc(rn_step, 1)
                dve.wait_ge(rn_step, base + 5)
                wait(dve, turned, k)
                dve.tensor_tensor(nbr[:, :, NROWS - 1], rn0[:, :], rtmp[:, :], ALU.mult).then_inc(rn_step, 1)
                dve.wait_ge(rn_step, base + 6)
                sk, n = skew[:, :, :], nbr[:, :, :]
                scale = bass.AP(n.tensor, n.offset + NROWS - 1, [list(n.ap[0]), [NROWS, BLOCKS], [0, S], [0, S]])
                for at, first, step_ in ((0, 0, 1), (BACK, REACH - 1, -1)):
                    src = bass.AP(sk.tensor, sk.offset + first,
                                  [list(sk.ap[0]), [REACH, BLOCKS], [step_, S], [step_ * WI, S]])
                    dst = bass.AP(n.tensor, n.offset + at, [list(n.ap[0]), [NROWS, BLOCKS], [S, S], [1, S]])
                    dve.tensor_tensor(dst, src, scale, ALU.mult).then_inc(rn_step, 1)

            def scale_weights(l):
                base = W_STEPS * l
                dve.wait_ge(w_in[l], 32)
                dve.tensor_reduce(wmax[:, l, :], w_raw[l], AX.X, ALU.max, apply_absolute_value=True
                                  ).then_inc(w_step, 1)
                dve.wait_ge(w_step, base + 1)
                dve.tensor_scalar(wmax[:, l, :], wmax[:, l, :], 2.0 ** -100, 2.0 ** 100, ALU.max, ALU.min
                                  ).then_inc(w_step, 1)
                dve.wait_ge(w_step, base + 2)
                bits = wmax[:, l, :].bitcast(I32)
                dve.tensor_scalar(bits, bits, 0x7F800000, None, ALU.bitwise_and).then_inc(w_step, 1)
                dve.wait_ge(w_step, base + 3)
                dve.reciprocal(wup[:, l, :], wmax[:, l, :]).then_inc(w_step, 1)
                dve.tensor_scalar(wdown[:, l, :], wmax[:, l, :], 1.0 / (W_SCALE * V_SCALE), None, ALU.mult
                                  ).then_inc(w_step, 1)
                dve.wait_ge(w_step, base + 4)
                for m in range(KT):
                    last = dve.tensor_scalar(w_raw[l][:, m, :], w_raw[l][:, m, :], wup[:, l, m:m + 1], W_SCALE,
                                             ALU.mult, ALU.mult)
                last.then_inc(w_step, 1)

            def low_weights(l):
                per = W_HIGHS
                for t in range(KT):
                    dve.wait_ge(w_high, per * l + t + 1)
                    dve.tensor_tensor(wl[:, l, t, :], conv_ps[:, t, :], wh[:, l, t, :], ALU.subtract
                                      ).then_inc(w_low, 1)
                dve.wait_ge(w_high, per * (l + 1))
                dve.tensor_tensor(wvol[64:64 + NS, l, :], turn_ps[0:NS, 1, :], wvol[0:NS, l, :], ALU.subtract
                                  ).then_inc(w_low, 1)

            def step(k, k0, i):
                u0, u = k0 - 1, k - 1
                if valid(u0):
                    correlation(k)
                if valid(k0 + 1):
                    unit_stats(k, k0, i)
                elif valid(u0):
                    volume_low(k)
                if k0 == 0:
                    for l in range(LAYERS):
                        scale_weights(l)
                for g in range(GROUPS):
                    if g == 2 and valid(k0 + 1):
                        unit_affine(k, k0)
                    if g == 2 and valid(k0):
                        norms(k)
                        neighbours(k)
                    if 3 <= g < 3 + KT and valid(k0 + 1):
                        low_tile(k, k0, g - 3)
                    if g == 7 and k0 == 0:
                        for l in range(LAYERS):
                            low_weights(l)
                    if g == 5 and valid(k0):
                        dve.wait_ge(turned, k + 1)
                        wait(dve, rows_out, 16 * k)
                        inner = rows[:, :].rearrange("s (h w) -> s h w", w=PW)[:, R:R + SPAN, R:R + WI]
                        dve.tensor_copy(inner, turn_ps[0:NROWS, 0, :].rearrange("s (h w) -> s h w", w=WI)
                                        ).then_inc(rows_v, 1)
                    if valid(u0):
                        m, n = g // 2, g % 2
                        xt = xs[:, ring_slot(unit_batch(u0) + 2 * i), m, n * HALF:(n + 1) * HALF]
                        dve.wait_ge(relu, GROUPS * u + g + 1)
                        dve.tensor_tensor(xt, xt, act_out[:, g % 2, :], ALU.add).then_inc(x_sum, 1)

            slots(dve, step)


_INS = ['x', 'L0_conv_conv_w', 'L0_conv_conv_b', 'L1_conv_conv_w', 'L1_conv_conv_b']


def kernel(**inputs):
    import numpy as _np
    import concourse.bacc as _bacc
    from concourse import mybir as _mybir
    from concourse.bass_utils import run_bass_kernel_spmd as _run

    nc = _bacc.Bacc("TRN2", target_bir_lowering=False, num_devices=1)
    arrays, args = {}, []
    for name in _INS:
        a = _np.ascontiguousarray(inputs[name])
        arrays[f"in_{name}_dram"] = a
        args.append(nc.dram_tensor(f"in_{name}_dram", a.shape, _mybir.dt.from_np(a.dtype), kind="ExternalInput").ap())
    x = arrays["in_x_dram"]
    out = nc.dram_tensor("out_0_dram", x.shape, _mybir.dt.from_np(x.dtype), kind="ExternalOutput").ap()
    build(nc, *args, out)
    r = _run(nc, [arrays], core_ids=[0])
    return r.results[0]["out_0_dram"]
```

```python
from contextlib import ExitStack

import concourse.bass as bass
from concourse import mybir

ALU = mybir.AluOpType
ACT = mybir.ActivationFunctionType
AX = mybir.AxisListType
F32 = mybir.dt.float32
F16 = mybir.dt.float16
I32 = mybir.dt.int32

P = 128
HALF = 512

BATCHES, LAYERS = 8, 2
UNITS = BATCHES * LAYERS
LEAD = 2
RING = 4

V_SCALE = 256.0
W_SCALE = 1024.0


def unit_layer(u):
    if u <= LEAD:
        return 0
    return 1 if u % 2 or u > UNITS - LEAD - 2 else 0


def unit_batch(u):
    if u <= LEAD:
        return u
    if unit_layer(u) == 0:
        return (u + LEAD) // 2
    return (u - LEAD - 1) // 2 if u < UNITS - LEAD else u - BATCHES


ORDER = [(unit_layer(u), unit_batch(u)) for u in range(UNITS)]
assert sorted(ORDER) == [(l, b) for l in range(LAYERS) for b in range(BATCHES)]

FIRST_LOOPED, PERIOD, TRIPS = 3, 4, 2
LAST_LOOPED = FIRST_LOOPED + PERIOD * TRIPS - 1
for _k in range(FIRST_LOOPED - 1, FIRST_LOOPED + PERIOD + 1):
    for _i in range(TRIPS):
        assert unit_layer(_k + PERIOD * _i) == unit_layer(_k)
        assert unit_batch(_k + PERIOD * _i) == unit_batch(_k) + _i * PERIOD // 2


def build(nc, x, w0, b0, w1, b1, out):
    B, C, HI, WI = x.shape
    PIX = HI * WI
    KT = C // P
    CI = w0.shape[1]
    S = 5
    R = S // 2
    NS = S * S
    GROUP = C // 32
    ROWS = P // WI
    BLOCKS = PIX // P
    BAND = (ROWS + 2 * R) * WI
    PAIRS = BLOCKS // 2
    REACH = 2 * R * WI + S
    CENTRE = R * WI + R
    SPAN = HALF // WI
    PW = WI + 2 * R
    PSZ = PW * (HI + 2 * R)
    BACK = 64
    NROWS = BACK + NS + 1
    MIR = (HI - 1) * PW + WI
    GPAD = 64
    GSZ = GPAD + BLOCKS * P * BAND + GPAD
    GROUPS = 2 * KT
    BN = 6
    assert (B, UNITS) == (BATCHES, B * LAYERS) and BAND * 2 == HALF

    weights = (w0, w1)
    biases = (b0, b1)
    x_v = x.rearrange("b (t p) h w -> b p t (h w)", p=P)
    out_v = out.rearrange("b (t p) h w -> b p t (h w)", p=P)

    ctx = ExitStack()
    with ctx:
        def sb(name, shape, dt):
            return ctx.enter_context(nc.sbuf_tensor(name, shape, dt))

        def ps(name, shape, dt):
            return ctx.enter_context(nc.psum_tensor(name, shape, dt))

        def sem(name):
            return ctx.enter_context(nc.semaphore(name))

        band_dram = nc.dram_tensor("band_dram", (2, GSZ), F32)
        rows_dram = nc.dram_tensor("rows_dram", (2, (NS + 1) * PSZ), F32)

        xs = sb("xs", [P, RING, KT, PIX], F32)
        opnd = sb("opnd", [P, RING, 2, KT, PIX], F16)
        wh = sb("wh", [P, LAYERS, KT, C], F16)
        whh = sb("whh", [P, LAYERS, KT, C], F16)
        wl = sb("wl", [P, LAYERS, KT, C], F16)
        wvol = sb("wvol", [P, LAYERS, C], F16)
        vol = sb("vol", [P, PIX], F16)
        v2 = sb("v2", [P, 2, PIX], F32)
        band = sb("band", [P, PAIRS, HALF], F32)
        skew = sb("skew", [P, BLOCKS, REACH], F32)
        nbr = sb("nbr", [P, BLOCKS, NROWS], F32)
        rows = sb("rows", [NROWS, PSZ], F32)
        mirror = sb("mirror", [NS, HI * PW], F32)
        rn_far = sb("rn_far", [NS, HI * PW], F32)
        rn_own = sb("rn_own", [NS, HI * PW], F32)
        corr = sb("corr", [NS, PIX], F32)
        act_out = sb("act_out", [P, 2, HALF], F32)
        ident = sb("ident", [P, P], F32)
        avg = sb("avg", [P, P], F32)
        stats = sb("stats", [P, KT, 2, BN], F32)
        mv = sb("mv", [P, KT, 2], F32)
        gmv = sb("gmv", [P, KT, 2], F32)
        gvar = sb("gvar", [P, KT], F32)
        gstd = sb("gstd", [P, KT], F32)
        grs = sb("grs", [P, KT], F32)
        gtmp = sb("gtmp", [P, KT], F32)
        affine = sb("affine", [P, 2, 2, KT], F32)
        nsq = sb("nsq", [P, BLOCKS], F32)
        nrm = sb("nrm", [P, BLOCKS], F32)
        rn0 = sb("rn0", [P, BLOCKS], F32)
        rtmp = sb("rtmp", [P, BLOCKS], F32)
        rn = sb("rn", [P, BLOCKS], F32)
        carrier = sb("carrier", [P, 16], F32)
        wmax = sb("wmax", [P, LAYERS, KT], F32)
        wup = sb("wup", [P, LAYERS, KT], F32)
        wdown = sb("wdown", [P, LAYERS, KT], F32)
        bias = sb("bias", [P, LAYERS, KT], F32)
        w_raw = [opnd[:, RING - LAYERS + l, :, :, :].rearrange("p a t n -> p (a t n)").bitcast(F32)
                 [:, 0:KT * CI].rearrange("p (t n) -> p t n", t=KT) for l in range(LAYERS)]

        conv_ps = ps("conv_ps", [P, 4, HALF], F32)
        gram_ps = ps("gram_ps", [P, 2, HALF], F32)
        turn_ps = ps("turn_ps", [P, 2, HALF], F32)

        const_step = sem("const_step")
        pads_out = sem("pads_out")
        w_in = [sem(f"w_in{l}") for l in range(LAYERS)]
        x_in = [[sem(f"x_in{q}_{t}") for t in range(KT)] for q in range(2)]
        x_out = [sem(f"x_out{t}") for t in range(KT)]
        w_step = sem("w_step")
        w_scaled = sem("w_scaled")
        w_turned = sem("w_turned")
        w_high = sem("w_high")
        w_half = sem("w_half")
        w_low = sem("w_low")
        bn_step = sem("bn_step")
        group_avg = sem("group_avg")
        gn_step = sem("gn_step")
        gn_root = sem("gn_root")
        high = sem("high")
        twice = sem("twice")
        low = sem("low")
        gram = sem("gram")
        band_sb = sem("band_sb")
        band_out = sem("band_out")
        skew_in = sem("skew_in")
        rn_step = sem("rn_step")
        rn_root = sem("rn_root")
        turned = sem("turned")
        rows_v = sem("rows_v")
        rows_a = sem("rows_a")
        rows_out = sem("rows_out")
        mirror_in = sem("mirror_in")
        corr_step = sem("corr_step")
        vol_high = sem("vol_high")
        vol_low = sem("vol_low")
        conv = sem("conv")
        relu = sem("relu")
        x_sum = sem("x_sum")

        CONSTS = 11
        BN_STEPS = KT + KT + 2
        GN_STEPS = 11
        RN_STEPS = 8
        CORR_STEPS = 3
        W_STEPS = 5
        W_HIGHS = KT + 2
        W_LOWS = KT + 1

        def wait(eng, s, value):
            if not isinstance(value, int) or value > 0:
                eng.wait_ge(s, value)

        def ring_slot(b):
            return b % RING

        def slots(eng, step):
            for k in range(-1, FIRST_LOOPED):
                step(k, k, 0)
            with eng.Fori(0, TRIPS) as i:
                for k0 in range(FIRST_LOOPED, FIRST_LOOPED + PERIOD):
                    step(k0 + PERIOD * i, k0, i)
            for k in range(LAST_LOOPED + 1, UNITS + 1):
                step(k, k, 0)

        def valid(u):
            return 0 <= u < UNITS

        def w_turned_at(l, n):
            return conv_ps[:, n, :] if l == 0 and n < KT else gram_ps[:, n % 2, :]

        FIRST_AT = lambda k0: 0 if k0 == 1 else 2
        V2_ON_POOL = (0, 1)
        AFFINE_AT = lambda k0: 0 if k0 > 1 else FIRST_AT(k0)
        NORM_AT = lambda k0: {0: 4, 1: 1}.get(k0, 2)
        TURN_AT = lambda k0: 5 if k0 == 0 else 4
        HOLD = 1
        W_AT = 3

        block = ctx.enter_context(nc.Block())

        @block.sync
        def _(sp):
            def load(b, slot, q):
                for t in range(KT):
                    sp.dma_start(xs[:, slot, t, :], x_v[b, :, t, :]).then_inc(x_in[q][t], 16)

            def load_weights(l):
                sp.dma_start(w_raw[l], weights[l].rearrange("(t p) c -> p t c", p=P)).then_inc(w_in[l], 16)
                with nc.allow_non_contiguous_dma(reason="512 bias values, once"):
                    sp.dma_start(bias[:, l, :], biases[l].rearrange("(t p) -> p t", p=P)).then_inc(w_in[l], 16)

            load(0, 0, 0)
            load(1, 1, 1)
            for l in range(LAYERS):
                load_weights(l)
            sp.wait_ge(const_step, CONSTS)
            for q in range(2):
                sp.dma_start(band_dram[q:q + 1, 0:GPAD], rows[0:1, 0:GPAD]).then_inc(pads_out, 16)
                sp.dma_start(band_dram[q:q + 1, GSZ - GPAD:GSZ], rows[0:1, 0:GPAD]).then_inc(pads_out, 16)
            sp.wait_ge(pads_out, 64)
            sp.wait_ge(bn_step, BN_STEPS)
            load(2, 2, 0)

            def tile_out(k, k0, i, t):
                b = unit_batch(k0 - 1) + 2 * i
                sp.wait_ge(x_sum, GROUPS * (k - 1) + 2 * t + 2)
                sp.dma_start(out_v[b, :, t, :], xs[:, ring_slot(b), t, :]).then_inc(x_out[t], 16)

            def tile_in(k, k0, i, t):
                b_0 = unit_batch(k0 - 1)
                b = b_0 + 2 * i
                if b_0 + RING < BATCHES:
                    sp.wait_ge(x_out[t], 16 * (b + 1))
                    sp.dma_start(xs[:, ring_slot(b), t, :], x_v[b + RING, :, t, :]).then_inc(x_in[b_0 % 2][t], 16)

            def band_through_dram(k, q):
                for p in range(PAIRS):
                    sp.wait_ge(band_sb, PAIRS * k + p + 1)
                    dst = bass.AP(band_dram, q * GSZ + GPAD + 2 * p * P * BAND,
                                  [[BAND, P], [P * BAND, 2], [1, BAND]])
                    sp.dma_start(dst, band[:, p, :].rearrange("p (a n) -> p a n", a=2)).then_inc(band_out, 16)
                sp.wait_ge(band_out, 16 * PAIRS * (k + 1))
                src = bass.AP(band_dram, q * GSZ + GPAD - R, [[BAND + 1, P], [P * BAND, BLOCKS], [1, REACH]])
                sp.dma_start(skew[:, :, :], src).then_inc(skew_in, 16)

            def rows_to_dram(k, q):
                sp.wait_ge(rows_v, k + 1)
                sp.wait_ge(rows_a, k + 1)
                sp.dma_start(rows_dram[q:q + 1, :].rearrange("a (s n) -> (a s) n", s=NS + 1),
                             rows[BACK:NROWS, :]).then_inc(rows_out, 16)

            def views_from_dram(k, q):
                sp.wait_ge(rows_out, 16 * (k + 1))
                base = q * (NS + 1) * PSZ
                sp.dma_start(mirror[:, 0:MIR],
                             bass.AP(rows_dram, base, [[S * PSZ + 1, S], [PSZ + PW, S], [1, MIR]])
                             ).then_inc(mirror_in, 16)
                sp.dma_start(rn_far[:, 0:MIR],
                             bass.AP(rows_dram, base + NS * PSZ, [[1, S], [PW, S], [1, MIR]])
                             ).then_inc(mirror_in, 16)
                sp.dma_start(rn_own[:, 0:MIR],
                             bass.AP(rows_dram, base + NS * PSZ + R * PW + R, [[0, NS], [1, MIR]])
                             ).then_inc(mirror_in, 16)

            def step(k, k0, i):
                finished = valid(k0 - 1) and unit_layer(k0 - 1) == 1
                if valid(k0):
                    band_through_dram(k, k0 % 2)
                if k0 == 0:
                    sp.wait_ge(bn_step, 2 * BN_STEPS)
                    load(3, 3, 1)
                if finished:
                    tile_out(k, k0, i, 0)
                    tile_in(k, k0, i, 0)
                    tile_out(k, k0, i, 1)
                if valid(k0):
                    rows_to_dram(k, k0 % 2)
                if finished:
                    tile_in(k, k0, i, 1)
                if valid(k0):
                    views_from_dram(k, k0 % 2)
                if finished:
                    for t in range(2, KT):
                        tile_out(k, k0, i, t)
                    for t in range(2, KT):
                        tile_in(k, k0, i, t)

            slots(sp, step)
            for t in range(KT):
                sp.wait_ge(x_out[t], 16 * BATCHES)

        @block.gpsimd
        def _(pool):
            pool.memset(ident[:, :], 0.0).then_inc(const_step, 1)
            pool.memset(avg[:, :], 1.0 / GROUP).then_inc(const_step, 1)
            pool.wait_ge(const_step, 2)
            pool.affine_select(out=ident[:, :], in_=ident[:, :], compare_op=ALU.not_equal, fill=1.0, base=0,
                               pattern=[[-1, P]], channel_multiplier=1).then_inc(const_step, 1)
            avg_v = avg[:, :].rearrange("p (g c) -> p g c", c=GROUP)
            pool.affine_select(out=avg_v, in_=avg_v, compare_op=ALU.is_ge, fill=0.0, base=0,
                               pattern=[[-GROUP, P // GROUP], [0, GROUP]], channel_multiplier=1
                               ).then_inc(const_step, 1)
            pool.wait_ge(const_step, 4)
            pool.affine_select(out=avg_v, in_=avg_v, compare_op=ALU.is_ge, fill=0.0, base=GROUP - 1,
                               pattern=[[GROUP, P // GROUP], [0, GROUP]], channel_multiplier=-1
                               ).then_inc(const_step, 1)
            pool.memset(rows[:, :], 0.0).then_inc(const_step, 1)
            pool.memset(band[:, 0, 0:R * WI], 0.0).then_inc(const_step, 1)
            pool.memset(band[:, PAIRS - 1, HALF - R * WI:HALF], 0.0).then_inc(const_step, 1)
            pool.memset(vol[:, :], 0.0).then_inc(const_step, 1)
            pool.memset(wvol[:, :, :], 0.0).then_inc(const_step, 1)
            pool.memset(nbr[:, :, NS:BACK], 0.0).then_inc(const_step, 1)
            def scaled_weights(l):
                pool.wait_ge(w_step, W_STEPS * (l + 1))
                for m in range(KT):
                    last = pool.tensor_scalar(w_raw[l][:, m, :], w_raw[l][:, m, :], wup[:, l, m:m + 1], W_SCALE,
                                              ALU.mult, ALU.mult)
                last.then_inc(w_scaled, 1)

            def half_weights(l):
                for t in range(KT):
                    pool.wait_ge(w_high, W_HIGHS * l + t + 1)
                    pool.tensor_scalar(whh[:, l, t, :], wh[:, l, t, :], 0.5, 1.0, ALU.mult, ALU.mult
                                       ).then_inc(w_half, 1)

            def correlation(k):
                own = rows[0:NS, :].rearrange("s (h w) -> s h w", w=PW)[:, R:R + HI, R:R + WI]
                mir, far, near = (a[:, :].rearrange("s (h w) -> s h w", w=PW)[:, :, 0:WI]
                                  for a in (mirror, rn_far, rn_own))
                dst = corr[:, :].rearrange("s (h w) -> s h w", w=WI)
                pool.wait_ge(mirror_in, 48 * (k + 1))
                pool.wait_ge(rows_v, k + 1)
                pool.wait_ge(rows_a, k + 1)
                pool.tensor_tensor(mir, mir, near, ALU.mult).then_inc(corr_step, 1)
                wait(pool, vol_low, k)
                wait(pool, vol_high, 2 * k)
                pool.tensor_tensor(dst, own, far, ALU.mult).then_inc(corr_step, 1)
                pool.wait_ge(corr_step, CORR_STEPS * k + 2)
                pool.tensor_tensor(dst, dst, mir, ALU.add).then_inc(corr_step, 1)

            def double_tiles(u):
                pool.wait_ge(gn_step, GN_STEPS * (u + 1))
                for t in range(KT):
                    wait(pool, low, KT * u + t - 1)
                    pool.tensor_scalar(v2[:, t % 2, :], xs[:, ring_slot(unit_batch(u)), t, :],
                                       affine[:, 1, 0, t:t + 1], affine[:, 1, 1, t:t + 1], ALU.mult, ALU.add
                                       ).then_inc(twice, 1)

            def step(k, k0, i):
                if k0 == 0:
                    scaled_weights(0)
                if k0 + 1 in V2_ON_POOL:
                    double_tiles(k0 + 1)
                if k0 == 0:
                    half_weights(0)
                if valid(k0):
                    correlation(k)
                if k0 == 0:
                    scaled_weights(1)
                    half_weights(1)

            slots(pool, step)


        @block.tensor
        def _(pe):
            pe.wait_ge(const_step, CONSTS)

            def average(u):
                pe.wait_ge(bn_step, BN_STEPS * (u + 1))
                wait(pe, rows_v, u - 1)
                pe.matmul(turn_ps[:, 0, 0:2 * KT], avg[:, :], mv[:, :, :].rearrange("p t s -> p (t s)"),
                          start=True, stop=True).then_inc(group_avg, 1)

            def turn_weights(l, n):
                pe.wait_ge(w_scaled, l + 1)
                bank = w_turned_at(l, n)
                if l == 0 and n == KT:
                    pe.wait_ge(band_sb, PAIRS * 2)
                if l == 1:
                    pe.wait_ge(w_low, W_LOWS + max(n - 1, 0))
                for m in range(KT):
                    cols = slice(n * P, (n + 1) * P) if n < KT else slice(C, CI)
                    last = pe.transpose(bank[0:cols.stop - cols.start, m * P:(m + 1) * P],
                                        w_raw[l][:, m, cols], ident[:, :])
                last.then_inc(w_turned, 1)

            def channels(u, slot, l, g):
                m, n = g // 2, g % 2
                wait(pe, relu, GROUPS * u + g - 3)
                for t in range(KT):
                    for w, part in ((wh, 0), (wl, 0), (whh, 1)):
                        pe.matmul(conv_ps[:, g % 4, :], w[:, l, t, m * P:(m + 1) * P],
                                  opnd[:, slot, part, t, n * HALF:(n + 1) * HALF],
                                  start=(t == 0 and w is wh), stop=False)

            def volume(l, g):
                m, n = g // 2, g % 2
                pe.matmul(conv_ps[:, g % 4, :], wvol[0:96, l, m * P:(m + 1) * P],
                          vol[0:96, n * HALF:(n + 1) * HALF], start=False, stop=True).then_inc(conv, 1)

            def step(k, k0, i):
                if valid(k0):
                    slot = k0 % RING
                    pe.wait_ge(high, KT * (k + 1))
                    pe.wait_ge(low, KT * (k + 1))
                    if k0 == 2:
                        pe.wait_ge(w_low, W_LOWS * LAYERS)
                    for p in range(PAIRS):
                        wait(pe, band_sb, PAIRS * k + p - 1)
                        for j in range(2 * p, 2 * p + 2):
                            r0 = max(ROWS * j - R, 0)
                            r1 = min(ROWS * (j + 1) + R, HI)
                            at = (j % 2) * BAND + (r0 - (ROWS * j - R)) * WI
                            for t in range(KT):
                                for part in range(2):
                                    last = pe.matmul(gram_ps[:, p % 2, at:at + (r1 - r0) * WI],
                                                     opnd[:, slot, 0, t, j * P:(j + 1) * P],
                                                     opnd[:, slot, part, t, r0 * WI:r1 * WI],
                                                     start=(t == 0 and part == 0),
                                                     stop=(t == KT - 1 and part == 1))
                        last.then_inc(gram, 1)
                u0 = k0 - 1
                if valid(u0):
                    u = k - 1
                    l = unit_layer(u0)
                    slot = u0 % RING
                for g in range(GROUPS):
                    if valid(k0 + 1) and g == (1 if k0 == 1 else 2):
                        average(k + 1)
                    if k0 == 0 and g == 3:
                        for n in range(KT):
                            turn_weights(0, n)
                    if k0 == 1 and g == 1:
                        turn_weights(0, KT)
                    if k0 == 1 and g >= W_AT:
                        turn_weights(1, g - W_AT)
                    if valid(k0) and g == TURN_AT(k0):
                        pe.wait_ge(rn_step, RN_STEPS * (k + 1))
                        if valid(k0 + 1):
                            pe.wait_ge(gn_step, GN_STEPS * (k + 1) + 1)
                        for j in range(BLOCKS):
                            last = pe.transpose(turn_ps[0:NROWS, j * P // HALF, j * P % HALF:j * P % HALF + P],
                                                nbr[:, j, :], ident[:, :])
                        last.then_inc(turned, 1)
                    if not valid(u0):
                        continue
                    if u0 in (0, LEAD + 1) and g == 0:
                        pe.wait_ge(w_half, KT * (l + 1))
                        pe.wait_ge(w_low, W_LOWS * l + KT)
                    channels(u, slot, l, g)
                    hold = 3 if u0 == UNITS - 1 else HOLD
                    if u0 in (0, LEAD + 1) and g == hold:
                        pe.wait_ge(w_low, W_LOWS * (l + 1))
                    if g == hold:
                        pe.wait_ge(vol_high, 2 * (u + 1))
                        pe.wait_ge(vol_low, u + 1)
                        for h in range(hold):
                            volume(l, h)
                    if g >= hold:
                        volume(l, g)

            slots(pe, step)

        @block.scalar
        def _(act):
            act.wait_ge(const_step, CONSTS)
            act.activation(carrier[:, 8:9], ident[:, 0:1], ACT.Sqrt)

            def high_weights(l, n):
                act.wait_ge(w_turned, (KT + 1) * l + n + 1)
                if n < KT:
                    act.activation(wh[:, l, n, :], w_turned_at(l, n), ACT.Copy).then_inc(w_high, 1)
                    return
                for at in (0, 32):
                    act.activation(wvol[at:at + NS, l, :], w_turned_at(l, n)[0:NS, :], ACT.Copy
                                   ).then_inc(w_high, 1)

            def norm_tile(u, u0, i, t):
                xt = xs[:, ring_slot(unit_batch(u0) + 2 * i), t, :]
                act.activation(opnd[:, u0 % RING, 0, t, :], xt, ACT.Identity, bias=affine[:, 0, 1, t:t + 1],
                               scale=affine[:, 0, 0, t:t + 1]).then_inc(high, 1)

            def volume_high(u):
                act.wait_ge(corr_step, CORR_STEPS * (u + 1))
                wait(act, conv, GROUPS * u)
                for at in (0, 64):
                    act.activation(vol[at:at + NS, :], corr[:, :], ACT.Copy, scale=V_SCALE / 2
                                   ).then_inc(vol_high, 1)

            def step(k, k0, i):
                u0, u = k0 - 1, k - 1
                for p in range(PAIRS):
                    if valid(k0):
                        act.wait_ge(gram, PAIRS * k + p + 1)
                        if p == 0:
                            wait(act, band_out, 16 * PAIRS * k)
                        a = R * WI if p == 0 else 0
                        z = HALF - (R * WI if p == PAIRS - 1 else 0)
                        act.activation(band[:, p, a:z], gram_ps[:, p % 2, a:z], ACT.Copy).then_inc(band_sb, 1)
                if valid(u0):
                    volume_high(u)
                if k0 == 1:
                    high_weights(0, KT)
                for g in range(GROUPS):
                    if k0 == 1 and g >= W_AT:
                        high_weights(1, g - W_AT)
                    if g == FIRST_AT(k0) and valid(k0 + 1):
                        act.wait_ge(gn_step, GN_STEPS * (k + 1) + 4)
                        act.activation(gstd[:, :], gvar[:, :], ACT.Sqrt).then_inc(gn_root, 1)
                    if g == NORM_AT(k0) and valid(k0):
                        act.wait_ge(rn_step, RN_STEPS * k + 1)
                        act.activation(nrm[:, :], nsq[:, :], ACT.Sqrt).then_inc(rn_root, 1)
                    t = g - FIRST_AT(k0)
                    if 0 <= t < KT and valid(k0 + 1):
                        if t == 0:
                            act.wait_ge(gn_step, GN_STEPS * (k + 2))
                        if k0 in (1, 2):
                            act.wait_ge(w_turned, (KT + 1) * k0)
                        norm_tile(k + 1, k0 + 1, i, t)
                    if k0 == 0 and g == 7:
                        for n in range(KT):
                            high_weights(0, n)
                    if g == TURN_AT(k0) and valid(k0):
                        act.wait_ge(turned, k + 1)
                        wait(act, rows_out, 16 * k)
                        wait(act, corr_step, CORR_STEPS * k)
                        inner = rows[:, :].rearrange("s (h w) -> s h w", w=PW)[:, R + SPAN:R + 2 * SPAN, R:R + WI]
                        act.activation(inner, turn_ps[0:NROWS, 1, :].rearrange("s (h w) -> s h w", w=WI),
                                       ACT.Copy).then_inc(rows_a, 1)
                    if valid(u0):
                        l = unit_layer(u0)
                        m = g // 2
                        act.wait_ge(conv, GROUPS * u + g + 1)
                        wait(act, x_sum, GROUPS * u + g - 1)
                        act.activation(act_out[:, g % 2, :], conv_ps[:, g % 4, :], ACT.Relu,
                                       bias=bias[:, l, m:m + 1], scale=wdown[:, l, m:m + 1]).then_inc(relu, 1)

            slots(act, step)

        @block.vector
        def _(dve):
            dve.wait_ge(const_step, CONSTS)

            def carry_dve(at):
                dve.memset(carrier[:, at:at + 1], 0.0)

            def unit_stats(k, k0, i):
                u, u0 = k + 1, k0 + 1
                b_0 = unit_batch(u0)
                slot = ring_slot(b_0 + 2 * i)
                base = BN_STEPS * u
                if unit_layer(u0) == 1:
                    wait(dve, x_sum, GROUPS * (u - 2))
                    if not isinstance(u, int):
                        carry_dve(KT)
                for t in range(KT):
                    if unit_layer(u0) == 0:
                        dve.wait_ge(x_in[b_0 % 2][t], 16 * (b_0 // 2 + 1 + i))
                        if not isinstance(u, int):
                            carry_dve(t)
                    for h in range(2):
                        last = dve.bn_stats(stats[:, t, h, :], xs[:, slot, t, h * HALF:(h + 1) * HALF])
                    last.then_inc(bn_step, 1)
                if k0 >= 0:
                    dve.wait_ge(group_avg, u)
                wait(dve, bn_step, base + KT)
                if not isinstance(u, int):
                    carry_dve(KT + 1)
                for t in range(KT):
                    dve.bn_aggr(mv[:, t, :], stats[:, t, :, :].rearrange("p h s -> p (h s)")).then_inc(bn_step, 1)
                dve.wait_ge(bn_step, base + 2 * KT)
                dve.tensor_tensor(gtmp[:, :], mv[:, :, 0], mv[:, :, 0], ALU.mult).then_inc(bn_step, 1)
                dve.wait_ge(bn_step, base + 2 * KT + 1)
                dve.tensor_tensor(mv[:, :, 1], mv[:, :, 1], gtmp[:, :], ALU.add).then_inc(bn_step, 1)
                if valid(k0 - 1):
                    volume_low(k)

            def unit_affine(k, k0):
                u = k + 1
                base = GN_STEPS * u
                dve.wait_ge(group_avg, u + 1)
                dve.tensor_copy(gmv[:, :, :].rearrange("p t s -> p (t s)"), turn_ps[:, 0, 0:2 * KT]
                                ).then_inc(gn_step, 1)
                dve.wait_ge(gn_step, base + 1)
                dve.tensor_tensor(gtmp[:, :], gmv[:, :, 0], gmv[:, :, 0], ALU.mult).then_inc(gn_step, 1)
                dve.wait_ge(gn_step, base + 2)
                dve.tensor_tensor(gvar[:, :], gmv[:, :, 1], gtmp[:, :], ALU.subtract).then_inc(gn_step, 1)
                dve.wait_ge(gn_step, base + 3)
                dve.tensor_scalar(gvar[:, :], gvar[:, :], 0.0, 1e-5, ALU.max, ALU.add).then_inc(gn_step, 1)
                dve.wait_ge(gn_root, u + 1)
                dve.reciprocal(grs[:, :], gstd[:, :]).then_inc(gn_step, 1)
                dve.wait_ge(gn_step, base + 5)
                dve.tensor_tensor(gtmp[:, :], grs[:, :], grs[:, :], ALU.mult).then_inc(gn_step, 1)
                dve.wait_ge(gn_step, base + 6)
                dve.tensor_tensor(gtmp[:, :], gtmp[:, :], gvar[:, :], ALU.mult).then_inc(gn_step, 1)
                dve.wait_ge(gn_step, base + 7)
                dve.tensor_scalar(gtmp[:, :], gtmp[:, :], -0.5, 1.5, ALU.mult, ALU.add).then_inc(gn_step, 1)
                dve.wait_ge(gn_step, base + 8)
                wait(dve, high, KT * u)
                dve.scalar_tensor_tensor(out=affine[:, 0, 0, :], in0=grs[:, :], scalar=V_SCALE, in1=gtmp[:, :],
                                         op0=ALU.mult, op1=ALU.mult).then_inc(gn_step, 1)
                dve.wait_ge(gn_step, base + 9)
                dve.scalar_tensor_tensor(out=affine[:, 0, 1, :], in0=gmv[:, :, 0], scalar=-1.0,
                                         in1=affine[:, 0, 0, :], op0=ALU.mult, op1=ALU.mult).then_inc(gn_step, 1)
                dve.wait_ge(gn_step, base + 10)
                dve.tensor_scalar(affine[:, 1, :, :], affine[:, 0, :, :], 2.0, None, ALU.mult).then_inc(gn_step, 1)

            def low_tile(k, k0, i, t):
                u, slot = k + 1, (k0 + 1) % RING
                dve.wait_ge(gn_step, GN_STEPS * (k + 2))
                if k0 + 1 not in V2_ON_POOL:
                    wait(dve, low, KT * u + t - 1)
                    dve.tensor_scalar(v2[:, t % 2, :], xs[:, ring_slot(unit_batch(k0 + 1) + 2 * i), t, :],
                                      affine[:, 1, 0, t:t + 1], affine[:, 1, 1, t:t + 1], ALU.mult, ALU.add
                                      ).then_inc(twice, 1)
                dve.wait_ge(high, KT * u + t + 1)
                dve.wait_ge(twice, KT * u + t + 1)
                dve.scalar_tensor_tensor(out=opnd[:, slot, 1, t, :], in0=opnd[:, slot, 0, t, :], scalar=-2.0,
                                         in1=v2[:, t % 2, :], op0=ALU.mult, op1=ALU.add).then_inc(low, 1)

            def volume_low(k):
                u = k - 1
                dve.wait_ge(vol_high, 2 * u + 1)
                dve.scalar_tensor_tensor(out=vol[32:32 + NS, :], in0=corr[:, :], scalar=V_SCALE / 2,
                                         in1=vol[0:NS, :], op0=ALU.mult, op1=ALU.subtract).then_inc(vol_low, 1)

            def norms(k):
                dve.wait_ge(skew_in, 16 * (k + 1))
                dve.tensor_scalar(nsq[:, :], skew[:, :, CENTRE], (V_SCALE * 1e-12) ** 2, None, ALU.max
                                  ).then_inc(rn_step, 1)

            def neighbours(k):
                base = RN_STEPS * k
                dve.wait_ge(rn_root, k + 1)
                dve.reciprocal(rn0[:, :], nrm[:, :]).then_inc(rn_step, 1)
                dve.wait_ge(rn_step, base + 2)
                dve.tensor_tensor(rtmp[:, :], rn0[:, :], rn0[:, :], ALU.mult).then_inc(rn_step, 1)
                dve.wait_ge(rn_step, base + 3)
                dve.tensor_tensor(rtmp[:, :], rtmp[:, :], nsq[:, :], ALU.mult).then_inc(rn_step, 1)
                dve.wait_ge(rn_step, base + 4)
                dve.tensor_scalar(rtmp[:, :], rtmp[:, :], -0.5, 1.5, ALU.mult, ALU.add).then_inc(rn_step, 1)
                dve.wait_ge(rn_step, base + 5)
                wait(dve, turned, k)
                dve.tensor_tensor(nbr[:, :, NROWS - 1], rn0[:, :], rtmp[:, :], ALU.mult).then_inc(rn_step, 1)
                dve.wait_ge(rn_step, base + 6)
                sk, n = skew[:, :, :], nbr[:, :, :]
                scale = bass.AP(n.tensor, n.offset + NROWS - 1, [list(n.ap[0]), [NROWS, BLOCKS], [0, S], [0, S]])
                for at, first, step_ in ((0, 0, 1), (BACK, REACH - 1, -1)):
                    src = bass.AP(sk.tensor, sk.offset + first,
                                  [list(sk.ap[0]), [REACH, BLOCKS], [step_, S], [step_ * WI, S]])
                    dst = bass.AP(n.tensor, n.offset + at, [list(n.ap[0]), [NROWS, BLOCKS], [S, S], [1, S]])
                    dve.tensor_tensor(dst, src, scale, ALU.mult).then_inc(rn_step, 1)

            def first_rows(k):
                dve.wait_ge(turned, k + 1)
                wait(dve, corr_step, CORR_STEPS * k)
                wait(dve, rows_out, 16 * k)
                inner = rows[:, :].rearrange("s (h w) -> s h w", w=PW)[:, R:R + SPAN, R:R + WI]
                dve.tensor_copy(inner, turn_ps[0:NROWS, 0, :].rearrange("s (h w) -> s h w", w=WI)
                                ).then_inc(rows_v, 1)

            def scale_weights(l):
                base = W_STEPS * l
                dve.wait_ge(w_in[l], 32)
                dve.tensor_reduce(wmax[:, l, :], w_raw[l], AX.X, ALU.max, apply_absolute_value=True
                                  ).then_inc(w_step, 1)
                dve.wait_ge(w_step, base + 1)
                dve.tensor_scalar(wmax[:, l, :], wmax[:, l, :], 2.0 ** -100, 2.0 ** 100, ALU.max, ALU.min
                                  ).then_inc(w_step, 1)
                dve.wait_ge(w_step, base + 2)
                bits = wmax[:, l, :].bitcast(I32)
                dve.tensor_scalar(bits, bits, 0x7F800000, None, ALU.bitwise_and).then_inc(w_step, 1)
                dve.wait_ge(w_step, base + 3)
                dve.reciprocal(wup[:, l, :], wmax[:, l, :]).then_inc(w_step, 1)
                dve.tensor_scalar(wdown[:, l, :], wmax[:, l, :], 1.0 / (W_SCALE * V_SCALE), None, ALU.mult
                                  ).then_inc(w_step, 1)
                dve.wait_ge(w_step, base + 4)

            def low_weights(l, n):
                if n < KT:
                    dve.wait_ge(w_high, W_HIGHS * l + n + 1)
                    dve.tensor_tensor(wl[:, l, n, :], w_turned_at(l, n), wh[:, l, n, :], ALU.subtract
                                      ).then_inc(w_low, 1)
                    return
                dve.wait_ge(w_high, W_HIGHS * (l + 1))
                dve.tensor_tensor(wvol[64:64 + NS, l, :], w_turned_at(l, n)[0:NS, :], wvol[0:NS, l, :],
                                  ALU.subtract).then_inc(w_low, 1)

            def step(k, k0, i):
                u0, u = k0 - 1, k - 1
                if valid(k0 + 1):
                    unit_stats(k, k0, i)
                elif valid(u0):
                    volume_low(k)
                if k0 == 0:
                    scale_weights(0)
                if k0 == 1:
                    low_weights(0, KT)
                for g in range(GROUPS):
                    if k0 == 1 and g >= W_AT:
                        low_weights(1, g - W_AT)
                    if g == AFFINE_AT(k0) and valid(k0 + 1):
                        unit_affine(k, k0)
                    if g == NORM_AT(k0) and valid(k0):
                        norms(k)
                        neighbours(k)
                    if k0 == 0 and g == TURN_AT(k0):
                        first_rows(k)
                    t = g - FIRST_AT(k0)
                    if 0 <= t < KT and valid(k0 + 1):
                        low_tile(k, k0, i, t)
                    if k0 == 0 and g == 7:
                        for n in range(KT):
                            low_weights(0, n)
                        scale_weights(1)
                    if k0 != 0 and g == TURN_AT(k0) and valid(k0):
                        first_rows(k)
                    if valid(u0):
                        m, n = g // 2, g % 2
                        xt = xs[:, ring_slot(unit_batch(u0) + 2 * i), m, n * HALF:(n + 1) * HALF]
                        dve.wait_ge(relu, GROUPS * u + g + 1)
                        dve.tensor_tensor(xt, xt, act_out[:, g % 2, :], ALU.add).then_inc(x_sum, 1)

            slots(dve, step)


_INS = ['x', 'L0_conv_conv_w', 'L0_conv_conv_b', 'L1_conv_conv_w', 'L1_conv_conv_b']


def kernel(**inputs):
    import numpy as _np
    import concourse.bacc as _bacc
    from concourse import mybir as _mybir
    from concourse.bass_utils import run_bass_kernel_spmd as _run

    nc = _bacc.Bacc("TRN2", target_bir_lowering=False, num_devices=1)
    arrays, args = {}, []
    for name in _INS:
        a = _np.ascontiguousarray(inputs[name])
        arrays[f"in_{name}_dram"] = a
        args.append(nc.dram_tensor(f"in_{name}_dram", a.shape, _mybir.dt.from_np(a.dtype), kind="ExternalInput").ap())
    x = arrays["in_x_dram"]
    out = nc.dram_tensor("out_0_dram", x.shape, _mybir.dt.from_np(x.dtype), kind="ExternalOutput").ap()
    build(nc, *args, out)
    r = _run(nc, [arrays], core_ids=[0])
    return r.results[0]["out_0_dram"]
```
